# Optimizing a Trainium2 kernel written in Bass

```python
import numpy as np
import jax
import jax.numpy as jnp

def _softmax(x, axis=-1):
    return jax.nn.softmax(x, axis=axis)

def _gelu(x):
    return jax.nn.gelu(x, approximate=True)

def _silu(x):
    return jax.nn.silu(x)

def _sigmoid(x):
    return jax.nn.sigmoid(x)

def _layernorm(x, axis=-1, eps=1e-05):
    m = jnp.mean(x, axis=axis, keepdims=True)
    v = jnp.var(x, axis=axis, keepdims=True)
    return (x - m) / jnp.sqrt(v + eps)

def _scatter_add(tgt, idx, src, axis=0):
    return tgt.at[idx].add(src)

def _segment_sum(src, seg, n):
    return jax.ops.segment_sum(src, seg, n)
kernel_name = 'mk_conv_preact_d1_conv_nchw512_r4_f3286a'

def setup_inputs(seed: int=0):
    np.random.seed(seed)
    _w = jnp.asarray

    def _rec_inputs():
        import jax
        import jax.numpy as jnp
        _gk = jax.random.key(seed)
        x = 7.22e-05 + 1 * jax.random.normal(jax.random.fold_in(_gk, 1), (4, 128, 16, 16), jnp.float32)
        return x
    x = _rec_inputs()

    def _L0_conv_setup():
        import jax, jax.numpy as jnp
        import numpy as np
        I_CH = 128
        O_CH = 250
        key = jax.random.key(seed)
        ks = jax.random.split(key, 7)
        B, C, H, W = (4, I_CH, 16, 16)
        x = jax.random.normal(ks[0], (B, C, H, W), dtype=jnp.float32)
        sc = 1.0 / np.sqrt(C)
        Wq = jax.random.uniform(ks[1], (O_CH, C), jnp.float32, -sc, sc)
        bq = jax.random.uniform(ks[2], (O_CH,), jnp.float32, -sc, sc)
        Wk = jax.random.uniform(ks[3], (O_CH, C), jnp.float32, -sc, sc)
        bk = jax.random.uniform(ks[4], (O_CH,), jnp.float32, -sc, sc)
        Wv = jax.random.uniform(ks[5], (C, C), jnp.float32, -sc, sc)
        bv = jax.random.uniform(ks[6], (C,), jnp.float32, -sc, sc)
        return {'x': x, 'Wq': Wq, 'bq': bq, 'Wk': Wk, 'bk': bk, 'Wv': Wv, 'bv': bv}
    _L0_conv_all = _L0_conv_setup()
    _L0_conv_in = {k: v for k, v in _L0_conv_all.items() if k in ('Wq', 'bq', 'Wk', 'bk', 'Wv', 'bv')}
    del _L0_conv_all
    return {'x': x, 'L0_conv_Wq': _L0_conv_in['Wq'], 'L0_conv_bq': _L0_conv_in['bq'], 'L0_conv_Wk': _L0_conv_in['Wk'], 'L0_conv_bk': _L0_conv_in['bk'], 'L0_conv_Wv': _L0_conv_in['Wv'], 'L0_conv_bv': _L0_conv_in['bv']}

def reference(x, L0_conv_Wq, L0_conv_bq, L0_conv_Wk, L0_conv_bk, L0_conv_Wv, L0_conv_bv):
    import jax
    import jax.numpy as jnp

    def _L0_conv_ref(x, Wq, bq, Wk, bk, Wv, bv):
        import jax, jax.numpy as jnp
        import numpy as np
        I_CH = 128
        O_CH = 250
        B, C, H, W = x.shape
        xf = x.reshape(B, C, H * W)
        q = jnp.einsum('bcn,oc->bon', xf, Wq) + bq[None, :, None]
        k = jnp.einsum('bcn,oc->bon', xf, Wk) + bk[None, :, None]
        v = jnp.einsum('bcn,oc->bon', xf, Wv) + bv[None, :, None]
        s = jnp.einsum('bon,bom->bnm', q, k)
        alpha = jax.nn.sigmoid(s)
        o = jnp.einsum('bcn,bnm->bcm', v, alpha)
        return o.reshape(B, C, H, W)

    def _gn(v, G=32, eps=1e-05):
        B_, C_, H_, W_ = v.shape
        g = v.reshape(B_, G, C_ // G, H_, W_)
        m = jnp.mean(g, axis=(2, 3, 4), keepdims=True)
        s = jnp.var(g, axis=(2, 3, 4), keepdims=True)
        return ((g - m) / jnp.sqrt(s + eps)).reshape(v.shape)

    def _ln_c(v, eps=1e-06):
        m = jnp.mean(v, axis=1, keepdims=True)
        s = jnp.var(v, axis=1, keepdims=True)
        return (v - m) / jnp.sqrt(s + eps)

    def _ln_t(v, eps=1e-05):
        m = jnp.mean(v, axis=-1, keepdims=True)
        s = jnp.var(v, axis=-1, keepdims=True)
        return (v - m) / jnp.sqrt(s + eps)

    def _to_tokens(v):
        B_, C_, H_, W_ = v.shape
        return v.reshape(B_, C_, H_ * W_).transpose(0, 2, 1)

    def _from_tokens(t, like):
        B_, C_, H_, W_ = like.shape
        return t.transpose(0, 2, 1).reshape(B_, C_, H_, W_)
    x = x + _L0_conv_ref(_gn(x), L0_conv_Wq, L0_conv_bq, L0_conv_Wk, L0_conv_bk, L0_conv_Wv, L0_conv_bv)
    return x

_drawn_inputs = setup_inputs


def setup_inputs(seed=0):
    import zlib

    import numpy as np

    out = dict(_drawn_inputs(seed))
    spreads = {}
    factors = {}
    for name, (base, spread) in spreads.items():
        noise = np.random.default_rng([zlib.crc32(name.encode()), seed]).standard_normal(out[name].shape)
        drawn = base * np.exp(spread * noise) if base else spread * noise
        out[name] = jnp.asarray(drawn.astype(out[name].dtype))
    for name, factor in factors.items():
        out[name] = (out[name] * factor).astype(out[name].dtype)
    return out
```

```python
import concourse.bass as bass
from concourse import mybir
from contextlib import ExitStack

F32 = mybir.dt.float32
I32 = mybir.dt.int32
ALU = mybir.AluOpType
ACT = mybir.ActivationFunctionType

B, C, N = 4, 128, 256
O = 250
ROWS = 2
GROUP = 4
EPS = 1e-5
P = 128
NT = N // P
QB, K0, KB = C, C + 1, 2 * C + 1
ROW = 2 * C + 2
WARM = 9


def attention_kernel(nc, x, wqk, wvT, bv, out):
    x_v = x.rearrange("b c h w -> c b (h w)")
    out_v = out.rearrange("b c h w -> c b (h w)")
    ctx = ExitStack()
    with ctx:
        def sb(name, shape, dt=F32):
            return ctx.enter_context(nc.sbuf_tensor(name, shape, dt))

        def sem(name):
            return ctx.enter_context(nc.semaphore(name))

        x_sb = sb("x_sb", [P, B, N])
        wqk_sb = sb("wqk_sb", [P, ROWS, ROW])
        wv_w = sb("wv_w", [P, C + 1])
        row_bias = sb("row_bias", [P, C + 1])
        a_sb = sb("a_sb", [P, C])
        u_sb = sb("u_sb", [P, 1])
        warm = sb("warm", [P, 512], mybir.dt.bfloat16)
        one = sb("one", [P, 1])
        stats = sb("stats", [P, B, 6])
        gstats = sb("gstats", [P, B, GROUP, 6])
        mv = sb("mv", [P, B, 2])
        nhv = sb("nhv", [P, B])
        rs = sb("rs", [P, B, 4])
        tmp = sb("tmp", [P, B])
        h_sb = sb("h_sb", [P, B, N])
        t_sb = sb("t_sb", [P, B, N])
        v_sb = sb("v_sb", [P, B, NT, C + 1])
        alpha = sb("alpha", [P, B, NT, N])
        out_sb = sb("out_sb", [P, B, N])
        dump = sb("dump", [P, 1])

        bank = [ctx.enter_context(nc.psum_tensor(f"bank{i}", [P, 512], F32)) for i in range(8)]
        s_ps = bank[0:4]
        t_ps, v_ps = bank[4], bank[5]
        o_ps = [bank[6], bank[7]]
        a_ps = bank[7]

        x_in = [sem(f"x_in{b}") for b in range(B)]
        wqk_in, wv_in, bv_in = sem("wqk_in"), sem("wv_in"), sem("bv_in")
        warm_set, one_set = sem("warm_set"), sem("one_set")
        fold_done, fold_sb = sem("fold_done"), sem("fold_sb")
        chain = sem("chain")
        h_ready = sem("h_ready")
        t_done, t_ready = sem("t_done"), sem("t_ready")
        v_done, v_ready = sem("v_done"), sem("v_ready")
        s_done, alpha_ready = sem("s_done"), sem("alpha_ready")
        o_done, out_ready, out_stored = sem("o_done"), sem("out_ready"), sem("out_stored")

        block = ctx.enter_context(nc.Block())

        @block.sync
        def _(sync):
            for b in range(B):
                sync.dma_start(x_sb[:, b, :], x_v[:, b, :]).then_inc(x_in[b], 16)
            for b in range(B):
                sync.wait_ge(out_ready, b + 1)
                sync.dma_start(out_v[:, b, :], out_sb[:, b, :]).then_inc(out_stored, 16)
            sync.wait_ge(out_stored, 16 * B)

        @block.gpsimd
        def _(pool):
            nc.gpsimd.memset(warm[:], 0.0).then_inc(warm_set, 1)
            nc.gpsimd.memset(one[:], 1.0).then_inc(one_set, 1)

        @block.scalar
        def _(act):
            act.dma_start(wqk_sb[:], wqk).then_inc(wqk_in, 16)
            act.dma_start(wv_w[:, 0:C], wvT).then_inc(wv_in, 16)
            act.dma_start(row_bias[:, 0:C], bv.rearrange("(o c) -> o c", o=1).to_broadcast([P, C])).then_inc(bv_in, 16)
            act.wait_ge(one_set, 1)
            nc.scalar.activation(dump[:], one[:], ACT.Sigmoid)
            act.wait_ge(fold_done, 1)
            nc.scalar.copy(a_sb[:], a_ps[:, 0:C]).then_inc(fold_sb, 1)
            nc.scalar.copy(wv_w[:, C:C + 1], a_ps[:, C:C + 1]).then_inc(fold_sb, 1)
            nc.scalar.copy(u_sb[:], a_ps[:, C + 1:C + 2]).then_inc(fold_sb, 1)
            nc.scalar.copy(row_bias[:, C:C + 1], a_ps[:, C + 2:C + 3]).then_inc(fold_sb, 1)
            act.wait_ge(fold_sb, 4)

            def evac_t(b):
                act.wait_ge(t_done, b + 1)
                nc.scalar.activation(t_sb[:, b, :], t_ps[:, 0:N], ACT.Identity, bias=u_sb[:, 0:1]).then_inc(t_ready, 1)

            evac_t(0)
            evac_t(1)
            for b in range(B):
                for t in range(NT):
                    i = NT * b + t
                    act.wait_ge(s_done, i + 1)
                    act.wait_ge(v_ready, b + 1)
                    nc.scalar.activation(alpha[:, b, t, :], s_ps[i % 4][:, 0:N], ACT.Sigmoid,
                                         bias=v_sb[:, b, t, C:C + 1]).then_inc(alpha_ready, 1)
                if b + 2 < B:
                    evac_t(b + 2)

        @block.vector
        def _(dve):
            done = [0]

            def step(ins):
                done[0] += 1
                ins.then_inc(chain, 1)
                dve.wait_ge(chain, done[0])

            def bn(b):
                dve.wait_ge(x_in[b], 16)
                step(nc.vector.bn_stats(stats[:, b, :], x_sb[:, b, :]))

            def norm(b0, b1):
                k = b1 - b0
                for g in range(GROUP):
                    nc.vector.stream_shuffle(gstats[:, b0:b1, g, :], stats[:, b0:b1, :],
                                             [GROUP * (p // GROUP) + g for p in range(32)]).then_inc(chain, 1)
                    done[0] += 1
                dve.wait_ge(chain, done[0])
                for b in range(b0, b1):
                    step(nc.vector.bn_aggr(mv[:, b, :], gstats[:, b, :, :].rearrange("p g s -> p (g s)")))
                var = mv[:, b0:b1, 1]
                step(nc.vector.tensor_scalar(nhv[:, b0:b1], var, EPS, -0.5, ALU.add, ALU.mult))
                step(nc.vector.tensor_scalar(tmp[:, b0:b1], var, EPS, None, ALU.add))
                step(nc.vector.tensor_scalar(rs[:, b0:b1, 0].bitcast(I32), tmp[:, b0:b1].bitcast(I32), -0.5, float(0x5f3759df),
                                             ALU.mult, ALU.add))
                for i in range(3):
                    y = rs[:, b0:b1, i]
                    if k == 1:
                        step(nc.vector.scalar_tensor_tensor(tmp[:, b0:b1], y, nhv[:, b0:b1], y, ALU.mult, ALU.mult))
                    else:
                        step(nc.vector.tensor_tensor(tmp[:, b0:b1], y, y, ALU.mult))
                        step(nc.vector.tensor_tensor(tmp[:, b0:b1], tmp[:, b0:b1], nhv[:, b0:b1], ALU.mult))
                    step(nc.vector.scalar_tensor_tensor(rs[:, b0:b1, i + 1], tmp[:, b0:b1], 1.5, y, ALU.add, ALU.mult))
                for b in range(b0, b1):
                    nc.vector.tensor_scalar(h_sb[:, b, :], x_sb[:, b, :], mv[:, b, 0:1], rs[:, b, 3:4],
                                            ALU.subtract, ALU.mult).then_inc(h_ready, 1)

            def evac_v(b):
                if b == 0:
                    dve.wait_ge(bv_in, 16)
                    dve.wait_ge(fold_sb, 4)
                dve.wait_ge(v_done, b + 1)
                nc.vector.tensor_tensor(v_sb[:, b, :, :], v_ps[:, 0:NT * (C + 1)].rearrange("p (t c) -> p t c", t=NT),
                                        row_bias[:].rearrange("p (o c) -> p o c", o=1).to_broadcast([P, NT, C + 1]), ALU.add).then_inc(v_ready, 1)

            def finish(b):
                dve.wait_ge(o_done, b + 1)
                nc.vector.tensor_tensor(out_sb[:, b, :], x_sb[:, b, :], o_ps[b % 2][:, 0:N], ALU.add).then_inc(out_ready, 1)

            bn(0)
            norm(0, 1)
            bn(1)
            norm(1, 2)
            evac_v(0)
            bn(2)
            bn(3)
            norm(2, 4)
            evac_v(1)
            finish(0)
            evac_v(2)
            finish(1)
            evac_v(3)
            finish(2)
            finish(3)

        @block.tensor
        def _(pe):
            pe.wait_ge(warm_set, 1)
            for _ in range(WARM):
                nc.tensor.matmul(t_ps[:, 0:512], warm[:, 0:P], warm[:, 0:512], start=True, stop=True)
            pe.wait_ge(wqk_in, 16)
            for j in range(ROWS):
                nc.tensor.matmul(a_ps[:, 0:C + 1], wqk_sb[:, j, 0:C], wqk_sb[:, j, K0:K0 + C + 1],
                                 start=(j == 0), stop=(j == ROWS - 1))
            for j in range(ROWS):
                nc.tensor.matmul(a_ps[:, C + 1:C + 2], wqk_sb[:, j, K0:KB], wqk_sb[:, j, QB:QB + 1],
                                 start=(j == 0), stop=(j == ROWS - 1))
            for j in range(ROWS):
                last = nc.tensor.matmul(a_ps[:, C + 2:C + 3], wqk_sb[:, j, QB:QB + 1].to_broadcast([P, P]),
                                        wqk_sb[:, j, KB:KB + 1], start=(j == 0), stop=(j == ROWS - 1))
            last.then_inc(fold_done, 1)
            pe.wait_ge(fold_sb, 4)
            pe.wait_ge(wv_in, 16)

            def tv(b):
                pe.wait_ge(h_ready, b + 1)
                if b >= 1:
                    pe.wait_ge(t_ready, b)
                nc.tensor.matmul(t_ps[:, 0:N], a_sb[:], h_sb[:, b, :], start=True, stop=True).then_inc(t_done, 1)
                if b >= 1:
                    pe.wait_ge(v_ready, b)
                for t in range(NT):
                    last = nc.tensor.matmul(v_ps[:, t * (C + 1):(t + 1) * (C + 1)], h_sb[:, b, t * P:(t + 1) * P],
                                            wv_w[:], start=True, stop=True)
                last.then_inc(v_done, 1)

            def scores(b):
                pe.wait_ge(t_ready, b + 1)
                for t in range(NT):
                    i = NT * b + t
                    if i >= 4:
                        pe.wait_ge(alpha_ready, i - 3)
                    nc.tensor.matmul(s_ps[i % 4][:, 0:N], t_sb[:, b, t * P:(t + 1) * P], h_sb[:, b, :],
                                     start=True, stop=True).then_inc(s_done, 1)

            def attend(b):
                if b >= 2:
                    pe.wait_ge(out_ready, b - 1)
                for t in range(NT):
                    pe.wait_ge(alpha_ready, NT * b + t + 1)
                    last = nc.tensor.matmul(o_ps[b % 2][:, 0:N], v_sb[:, b, t, 0:C], alpha[:, b, t, :],
                                            start=(t == 0), stop=(t == NT - 1))
                last.then_inc(o_done, 1)

            tv(0)
            scores(0)
            for b in range(1, B):
                tv(b)
                scores(b)
                attend(b - 1)
            attend(B - 1)


def kernel(x, L0_conv_Wq, L0_conv_bq, L0_conv_Wk, L0_conv_bk, L0_conv_Wv, L0_conv_bv):
    import numpy as np
    import concourse.bacc as bacc
    from concourse.bass_utils import run_bass_kernel_spmd

    wqk = np.zeros((P * ROWS, ROW), np.float32)
    wqk[:O, 0:C] = L0_conv_Wq
    wqk[:O, QB] = L0_conv_bq
    wqk[:O, K0:KB] = L0_conv_Wk
    wqk[:O, KB] = L0_conv_bk
    arrays = {
        "x": np.ascontiguousarray(x),
        "wqk": wqk.reshape(P, ROWS, ROW),
        "wvT": np.ascontiguousarray(np.asarray(L0_conv_Wv).T),
        "bv": np.ascontiguousarray(L0_conv_bv),
    }
    nc = bacc.Bacc("TRN2", target_bir_lowering=False, num_devices=1)
    ins = [nc.dram_tensor(n, a.shape, mybir.dt.from_np(a.dtype), kind="ExternalInput").ap() for n, a in arrays.items()]
    out = nc.dram_tensor("out", arrays["x"].shape, F32, kind="ExternalOutput").ap()
    attention_kernel(nc, *ins, out)
    return run_bass_kernel_spmd(nc, [arrays], core_ids=[0]).results[0]["out"]
```

```python
import concourse.bass as bass
from concourse import mybir
from contextlib import ExitStack


F32 = mybir.dt.float32
F32R = mybir.dt.float32r
BF16 = mybir.dt.bfloat16
ALU = mybir.AluOpType
ACT = mybir.ActivationFunctionType

P = 128
B, C, N = 4, 128, 256
O = 250
ROWS = 2
GROUP = 4
EPS = 1e-5
NT = N // P
WQ, BQ, WK, BK = 0, C, C + 1, 2 * C + 1
ROW = 2 * C + 2
VC = C + 1
STATS = 6
WARM_PRODUCTS = 14

WARM_BANK = 0
FOLD_BANK, BIAS_BANK = 6, 7
T0_BANKS = [3, 4]
T_BANK = [None, 3, 4, 3]
V_BANK = [5, 7, 5, 7]
S_BANK = [0, 1, 2, 0, 1, 2, 0, 4]
O_BANK = [6, 6, 5]
LAST_BANKS = [6, 7]


def attention_kernel(nc, x, wqk, wvT, bv, out):
    x_v = x.rearrange("b c h w -> c b (h w)")
    out_v = out.rearrange("b c h w -> c b (h w)")

    def half(t):
        return slice(t * P, (t + 1) * P)

    ctx = ExitStack()
    with ctx:
        def sb(name, shape, dt=F32):
            return ctx.enter_context(nc.sbuf_tensor(name, shape, dt))

        def sem(name):
            return ctx.enter_context(nc.semaphore(name))

        x_sb = sb("x_sb", [P, B, N])
        wqk_sb = sb("wqk_sb", [P, ROWS, ROW])
        a_sb = sb("a_sb", [P, C])
        wv_sb = sb("wv_sb", [P, VC])
        row_bias = sb("row_bias", [P, VC])
        u_sb = sb("u_sb", [P, 1])
        minus_half = sb("minus_half", [P, B])
        table_dump = sb("table_dump", [P, 1])
        group_stats = sb("group_stats", [P, B, GROUP, STATS])
        moments = sb("moments", [P, B, 2])
        var_eps = sb("var_eps", [P, B])
        rstd = sb("rstd", [P, B])
        h_sb = sb("h_sb", [P, B, N])
        h_hi, h_lo = sb("h_hi", [P, B, N], F32R), sb("h_lo", [P, B, N], F32R)
        t_sb = sb("t_sb", [P, N])
        t_hi, t_lo = sb("t_hi", [P, B, N], F32R), sb("t_lo", [P, B, N], F32R)
        v_sb = sb("v_sb", [P, B, NT, VC])
        alpha = sb("alpha", [P, B, NT, N])
        out_sb = sb("out_sb", [P, B, N])
        bank = [ctx.enter_context(nc.psum_tensor(f"bank{i}", [P, 512], F32)) for i in range(8)]

        x_in = [sem("x_in0"), sem("x_in1"), sem("x_in23")]
        wqk_in, wv_in, bv_in = sem("wqk_in"), sem("wv_in"), sem("bv_in")
        const_set = sem("const_set")
        fold_done, bias_done = sem("fold_done"), sem("bias_done")
        a_ready, w_ready = sem("a_ready"), sem("w_ready")
        u_ready, c0_ready = sem("u_ready"), sem("c0_ready")
        stats_ready = sem("stats_ready")
        moments_ready, var_ready, rstd_ready = sem("moments_ready"), sem("var_ready"), sem("rstd_ready")
        h_ready, h_hi_ready, h_lo_ready = sem("h_ready"), sem("h_hi_ready"), sem("h_lo_ready")
        t_done, t0_ready = sem("t_done"), sem("t0_ready")
        t_hi_ready, t_lo_ready = sem("t_hi_ready"), sem("t_lo_ready")
        v_done, v_ready = sem("v_done"), sem("v_ready")
        s_done, alpha_ready = sem("s_done"), sem("alpha_ready")
        o_done, out_ready, out_stored = sem("o_done"), sem("out_ready"), sem("out_stored")

        block = ctx.enter_context(nc.Block())

        @block.sync
        def _(sync):
            sync.dma_start(x_sb[:, 0, :], x_v[:, 0, :]).then_inc(x_in[0], 16)
            sync.dma_start(wqk_sb[:], wqk).then_inc(wqk_in, 16)
            sync.dma_start(x_sb[:, 1, :], x_v[:, 1, :]).then_inc(x_in[1], 16)
            sync.dma_start(wv_sb[:, 0:C], wvT).then_inc(wv_in, 16)
            sync.dma_start(x_sb[:, 2:B, :], x_v[:, 2:B, :]).then_inc(x_in[2], 16)
            sync.dma_start(row_bias[:, 0:C],
                           bv.rearrange("(o c) -> o c", o=1).to_broadcast([P, C])).then_inc(bv_in, 16)
            for b in range(B - 1):
                sync.wait_ge(out_ready, b + 1)
                sync.dma_start(out_v[:, b, :], out_sb[:, b, :]).then_inc(out_stored, 16)
            for t in range(NT):
                sync.wait_ge(out_ready, B + t)
                sync.dma_start(out_v[:, B - 1, half(t)], out_sb[:, B - 1, half(t)]).then_inc(out_stored, 16)
            sync.wait_ge(out_stored, 16 * (B - 1 + NT))

        @block.gpsimd
        def _(pool):
            nc.gpsimd.memset(minus_half[:], -0.5).then_inc(const_set, 1)

            def inverse_deviation(b0, b1, call):
                pool.wait_ge(const_set, 1)
                pool.wait_ge(var_ready, call)
                nc.gpsimd.tensor_tensor(rstd[:, b0:b1], var_eps[:, b0:b1], minus_half[:, b0:b1],
                                        ALU.pow).then_inc(rstd_ready, 1)

            def low_part_of_h(b):
                pool.wait_ge(h_hi_ready, b)
                nc.gpsimd.tensor_tensor(h_lo[:, b, :], h_sb[:, b, :], h_hi[:, b, :].bitcast(F32),
                                        ALU.subtract).then_inc(h_lo_ready, 1)

            inverse_deviation(0, 1, 1)
            inverse_deviation(1, 2, 2)
            inverse_deviation(2, 4, 3)
            low_part_of_h(2)
            low_part_of_h(3)

        @block.scalar
        def _(act):
            act.wait_ge(const_set, 1)
            nc.scalar.activation(table_dump[:], minus_half[:, 0:1], ACT.Sigmoid)

            act.wait_ge(fold_done, 1)
            nc.scalar.copy(a_sb[:], bank[FOLD_BANK][:, 0:C]).then_inc(a_ready, 1)
            nc.scalar.copy(wv_sb[:, C:VC], bank[FOLD_BANK][:, C:C + 1]).then_inc(w_ready, 1)
            act.wait_ge(bias_done, 1)
            nc.scalar.copy(u_sb[:], bank[BIAS_BANK][:, 0:1]).then_inc(u_ready, 1)
            nc.scalar.copy(row_bias[:, C:VC], bank[BIAS_BANK][:, 1:2]).then_inc(c0_ready, 1)
            act.wait_ge(u_ready, 1)
            for t in range(NT):
                act.wait_ge(t_done, t + 1)
                nc.scalar.activation(t_sb[:, half(t)], bank[T0_BANKS[t]][:, 0:P], ACT.Identity,
                                     bias=u_sb[:, 0:1]).then_inc(t0_ready, 1)

            def high_part_of_h(b):
                act.wait_ge(h_ready, b + 1)
                nc.scalar.copy(h_hi[:, b, :], h_sb[:, b, :]).then_inc(h_hi_ready, 1)

            def high_part_of_t(b):
                act.wait_ge(t_done, NT + b)
                nc.scalar.activation(t_hi[:, b, :], bank[T_BANK[b]][:, 0:N], ACT.Identity,
                                     bias=u_sb[:, 0:1]).then_inc(t_hi_ready, 1)

            def sigmoid(b, t):
                act.wait_ge(v_ready, b + 1)
                act.wait_ge(s_done, NT * b + t + 1)
                nc.scalar.activation(alpha[:, b, t, :], bank[S_BANK[NT * b + t]][:, 0:N], ACT.Sigmoid,
                                     bias=v_sb[:, b, t, C:VC]).then_inc(alpha_ready, 1)

            high_part_of_h(1)
            sigmoid(0, 0)
            sigmoid(0, 1)
            high_part_of_t(1)
            high_part_of_h(2)
            high_part_of_h(3)
            sigmoid(1, 0)
            sigmoid(1, 1)
            high_part_of_t(2)
            high_part_of_t(3)
            for b in (2, 3):
                for t in range(NT):
                    sigmoid(b, t)

        @block.vector
        def _(dve):
            marked = [0]

            def mark(instruction):
                marked[0] += 1
                instruction.then_inc(stats_ready, 1)

            def channel_stats(b):
                dve.wait_ge(x_in[min(b, 2)], 16)
                mark(nc.vector.bn_stats(group_stats[:, b, 0, :], x_sb[:, b, :]))

            def gather_group(b0, b1):
                dve.wait_ge(stats_ready, marked[0])
                for g in range(1, GROUP):
                    mark(nc.vector.stream_shuffle(group_stats[:, b0:b1, g, :], group_stats[:, b0:b1, 0, :],
                                                  [p ^ g for p in range(32)]))

            def group_moments(b0, b1):
                dve.wait_ge(stats_ready, marked[0])
                for b in range(b0, b1):
                    nc.vector.bn_aggr(moments[:, b, :],
                                      group_stats[:, b, :, :].rearrange("p g s -> p (g s)")).then_inc(moments_ready, 1)
                dve.wait_ge(moments_ready, b1)
                nc.vector.tensor_scalar(var_eps[:, b0:b1], moments[:, b0:b1, 1], EPS, None,
                                        ALU.add).then_inc(var_ready, 1)

            def normalize(b, call):
                dve.wait_ge(rstd_ready, call)
                nc.vector.tensor_scalar(h_sb[:, b, :], x_sb[:, b, :], moments[:, b, 0:1], rstd[:, b:b + 1],
                                        ALU.subtract, ALU.mult).then_inc(h_ready, 1)

            def low_part_of_t(b):
                dve.wait_ge(t_hi_ready, b)
                nc.vector.scalar_tensor_tensor(t_lo[:, b, :], bank[T_BANK[b]][:, 0:N], u_sb[:, 0:1],
                                               t_hi[:, b, :].bitcast(F32), ALU.add, ALU.subtract).then_inc(t_lo_ready, 1)

            def values(b):
                dve.wait_ge(v_done, b + 1)
                nc.vector.tensor_tensor(v_sb[:, b, :, :],
                                        bank[V_BANK[b]][:, 0:NT * VC].rearrange("p (t c) -> p t c", t=NT),
                                        row_bias[:].rearrange("p (o c) -> p o c", o=1).to_broadcast([P, NT, VC]),
                                        ALU.add).then_inc(v_ready, 1)

            def residual(b):
                dve.wait_ge(o_done, b + 1)
                nc.vector.tensor_tensor(out_sb[:, b, :], x_sb[:, b, :], bank[O_BANK[b]][:, 0:N],
                                        ALU.add).then_inc(out_ready, 1)

            channel_stats(0)
            gather_group(0, 1)
            group_moments(0, 1)
            channel_stats(1)
            normalize(0, 1)
            gather_group(1, 2)
            group_moments(1, 2)
            channel_stats(2)
            channel_stats(3)
            normalize(1, 2)
            dve.wait_ge(bv_in, 16)
            dve.wait_ge(c0_ready, 1)
            values(0)
            gather_group(2, 4)
            group_moments(2, 4)
            dve.wait_ge(h_hi_ready, 1)
            nc.vector.tensor_tensor(h_lo[:, 1, :], h_sb[:, 1, :], h_hi[:, 1, :].bitcast(F32),
                                    ALU.subtract).then_inc(h_lo_ready, 1)
            low_part_of_t(1)
            normalize(2, 3)
            values(1)
            normalize(3, 3)
            residual(0)
            low_part_of_t(2)
            values(2)
            low_part_of_t(3)
            values(3)
            residual(1)
            residual(2)
            for t in range(NT):
                dve.wait_ge(o_done, B + t)
                nc.vector.tensor_tensor(out_sb[:, B - 1, half(t)], x_sb[:, B - 1, half(t)],
                                        bank[LAST_BANKS[t]][:, 0:P], ALU.add).then_inc(out_ready, 1)

        @block.tensor
        def _(pe):
            zero = nc.const_aps.tensor(0.0, [P, 1], F32).bitcast(BF16)[:, 0:1]
            for _ in range(WARM_PRODUCTS):
                nc.tensor.matmul(bank[WARM_BANK][:, 0:N], zero.to_broadcast([P, P]), zero.to_broadcast([P, N]),
                                 start=True, stop=True)

            pe.wait_ge(wqk_in, 16)
            for j in range(ROWS):
                last = nc.tensor.matmul(bank[FOLD_BANK][:, 0:C + 1], wqk_sb[:, j, WQ:WQ + C], wqk_sb[:, j, WK:WK + C + 1],
                                        start=(j == 0), stop=(j == ROWS - 1))
            last.then_inc(fold_done, 1)
            for j in range(ROWS):
                nc.tensor.matmul(bank[BIAS_BANK][:, 0:1], wqk_sb[:, j, WK:WK + C], wqk_sb[:, j, BQ:BQ + 1],
                                 start=(j == 0), stop=(j == ROWS - 1))
            for j in range(ROWS):
                last = nc.tensor.matmul(bank[BIAS_BANK][:, 1:2], wqk_sb[:, j, BQ:BQ + 1].to_broadcast([P, P]),
                                        wqk_sb[:, j, BK:BK + 1], start=(j == 0), stop=(j == ROWS - 1))
            last.then_inc(bias_done, 1)

            def project_values(b):
                for t in range(NT):
                    last = nc.tensor.matmul(bank[V_BANK[b]][:, t * VC:(t + 1) * VC], h_sb[:, b, half(t)], wv_sb[:],
                                            start=True, stop=True)
                last.then_inc(v_done, 1)

            def project(b):
                pe.wait_ge(h_ready, b + 1)
                if b == 3:
                    pe.wait_ge(t_lo_ready, 1)
                nc.tensor.matmul(bank[T_BANK[b]][:, 0:N], a_sb[:], h_sb[:, b, :], start=True, stop=True).then_inc(t_done, 1)
                if b >= 2:
                    pe.wait_ge(v_ready, b - 1)
                project_values(b)

            def scores(b):
                pe.wait_ge(t_hi_ready, b)
                pe.wait_ge(h_lo_ready, b)
                for t in range(NT):
                    i = NT * b + t
                    if S_BANK[i] in S_BANK[:i]:
                        before = max(j for j in range(i) if S_BANK[j] == S_BANK[i])
                        pe.wait_ge(alpha_ready, before + 1)
                    s_out = bank[S_BANK[i]][:, 0:N]
                    nc.tensor.matmul(s_out, t_hi[:, b, half(t)], h_hi[:, b, :], start=True, stop=False)
                    nc.tensor.matmul(s_out, t_hi[:, b, half(t)], h_lo[:, b, :], start=False, stop=False)
                    if t == 0:
                        pe.wait_ge(t_lo_ready, b)
                    nc.tensor.matmul(s_out, t_lo[:, b, half(t)], h_hi[:, b, :], start=False, stop=True).then_inc(s_done, 1)

            def attend(b, o_out, columns):
                for t in range(NT):
                    pe.wait_ge(alpha_ready, NT * b + t + 1)
                    last = nc.tensor.matmul(o_out, v_sb[:, b, t, 0:C], alpha[:, b, t, columns],
                                            start=(t == 0), stop=(t == NT - 1))
                last.then_inc(o_done, 1)

            pe.wait_ge(a_ready, 1)
            pe.wait_ge(h_ready, 1)
            for t in range(NT):
                nc.tensor.matmul(bank[T0_BANKS[t]][:, 0:P], a_sb[:], h_sb[:, 0, half(t)],
                                 start=True, stop=True).then_inc(t_done, 1)
            pe.wait_ge(wv_in, 16)
            pe.wait_ge(w_ready, 1)
            project_values(0)
            for t in range(NT):
                pe.wait_ge(t0_ready, t + 1)
                nc.tensor.matmul(bank[S_BANK[t]][:, 0:N], t_sb[:, half(t)], h_sb[:, 0, :],
                                 start=True, stop=True).then_inc(s_done, 1)

            everything = slice(0, N)
            pe.wait_ge(c0_ready, 1)
            project(1)
            attend(0, bank[O_BANK[0]][:, 0:N], everything)
            scores(1)
            project(2)
            project(3)
            pe.wait_ge(out_ready, 1)
            attend(1, bank[O_BANK[1]][:, 0:N], everything)
            scores(2)
            scores(3)
            pe.wait_ge(v_ready, 3)
            attend(2, bank[O_BANK[2]][:, 0:N], everything)
            pe.wait_ge(out_ready, 2)
            pe.wait_ge(v_ready, 4)
            for m in range(NT):
                attend(B - 1, bank[LAST_BANKS[m]][:, 0:P], half(m))


def kernel(x, L0_conv_Wq, L0_conv_bq, L0_conv_Wk, L0_conv_bk, L0_conv_Wv, L0_conv_bv):
    import numpy as np
    import concourse.bacc as bacc
    from concourse.bass_utils import run_bass_kernel_spmd

    wqk = np.zeros((P * ROWS, ROW), np.float32)
    wqk[:O, WQ:WQ + C] = L0_conv_Wq
    wqk[:O, BQ] = L0_conv_bq
    wqk[:O, WK:WK + C] = L0_conv_Wk
    wqk[:O, BK] = L0_conv_bk
    arrays = {
        "x": np.ascontiguousarray(x),
        "wqk": wqk.reshape(P, ROWS, ROW),
        "wvT": np.ascontiguousarray(np.asarray(L0_conv_Wv).T),
        "bv": np.ascontiguousarray(L0_conv_bv),
    }
    nc = bacc.Bacc("TRN2", target_bir_lowering=False, num_devices=1)
    ins = [nc.dram_tensor(n, a.shape, mybir.dt.from_np(a.dtype), kind="ExternalInput").ap() for n, a in arrays.items()]
    out = nc.dram_tensor("out", arrays["x"].shape, F32, kind="ExternalOutput").ap()
    attention_kernel(nc, *ins, out)
    return run_bass_kernel_spmd(nc, [arrays], core_ids=[0]).results[0]["out"]
```
